# Optimizing a Trainium2 kernel written in Bass

```python
import numpy as np
import jax
import jax.numpy as jnp

def _softmax(x, axis=-1):
    return jax.nn.softmax(x, axis=axis)

def _gelu(x):
    return jax.nn.gelu(x, approximate=True)

def _silu(x):
    return jax.nn.silu(x)

def _sigmoid(x):
    return jax.nn.sigmoid(x)

def _layernorm(x, axis=-1, eps=1e-05):
    m = jnp.mean(x, axis=axis, keepdims=True)
    v = jnp.var(x, axis=axis, keepdims=True)
    return (x - m) / jnp.sqrt(v + eps)

def _scatter_add(tgt, idx, src, axis=0):
    return tgt.at[idx].add(src)

def _segment_sum(src, seg, n):
    return jax.ops.segment_sum(src, seg, n)
kernel_name = 'mk_dlrm_tower_d1_rec_r8_e14902'

def setup_inputs(seed: int=0):
    np.random.seed(seed)
    _w = jnp.asarray

    def _rec_inputs():
        import jax
        import jax.numpy as jnp
        _tk = jax.random.key(seed)
        ids = jnp.stack([jax.random.randint(jax.random.fold_in(_tk, 200 + f), (2048,), 0, v, jnp.int32) for f, v in enumerate([1250, 1250, 1250, 1250, 12500, 12500, 1000, 125000, 1250, 12500, 12500, 12500, 1000, 1250, 12500, 1250, 1000, 1000, 1000, 1000, 12500, 1250, 12500, 1000, 1000, 1250, 1250, 1250, 1250, 1000, 1250, 1250, 1000])], axis=1)
        tbl_0 = 0.05 * jax.random.normal(jax.random.fold_in(_tk, 500 + 0), (1250, 128), jnp.float32)
        tbl_1 = 0.05 * jax.random.normal(jax.random.fold_in(_tk, 500 + 1), (1250, 128), jnp.float32)
        tbl_2 = 0.05 * jax.random.normal(jax.random.fold_in(_tk, 500 + 2), (1250, 128), jnp.float32)
        tbl_3 = 0.05 * jax.random.normal(jax.random.fold_in(_tk, 500 + 3), (1250, 128), jnp.float32)
        tbl_4 = 0.05 * jax.random.normal(jax.random.fold_in(_tk, 500 + 4), (12500, 128), jnp.float32)
        tbl_5 = 0.05 * jax.random.normal(jax.random.fold_in(_tk, 500 + 5), (12500, 128), jnp.float32)
        tbl_6 = 0.05 * jax.random.normal(jax.random.fold_in(_tk, 500 + 6), (1000, 128), jnp.float32)
        tbl_7 = 0.05 * jax.random.normal(jax.random.fold_in(_tk, 500 + 7), (125000, 128), jnp.float32)
        tbl_8 = 0.05 * jax.random.normal(jax.random.fold_in(_tk, 500 + 8), (1250, 128), jnp.float32)
        tbl_9 = 0.05 * jax.random.normal(jax.random.fold_in(_tk, 500 + 9), (12500, 128), jnp.float32)
        tbl_10 = 0.05 * jax.random.normal(jax.random.fold_in(_tk, 500 + 10), (12500, 128), jnp.float32)
        tbl_11 = 0.05 * jax.random.normal(jax.random.fold_in(_tk, 500 + 11), (12500, 128), jnp.float32)
        tbl_12 = 0.05 * jax.random.normal(jax.random.fold_in(_tk, 500 + 12), (1000, 128), jnp.float32)
        tbl_13 = 0.05 * jax.random.normal(jax.random.fold_in(_tk, 500 + 13), (1250, 128), jnp.float32)
        tbl_14 = 0.05 * jax.random.normal(jax.random.fold_in(_tk, 500 + 14), (12500, 128), jnp.float32)
        tbl_15 = 0.05 * jax.random.normal(jax.random.fold_in(_tk, 500 + 15), (1250, 128), jnp.float32)
        tbl_16 = 0.05 * jax.random.normal(jax.random.fold_in(_tk, 500 + 16), (1000, 128), jnp.float32)
        tbl_17 = 0.05 * jax.random.normal(jax.random.fold_in(_tk, 500 + 17), (1000, 128), jnp.float32)
        tbl_18 = 0.05 * jax.random.normal(jax.random.fold_in(_tk, 500 + 18), (1000, 128), jnp.float32)
        tbl_19 = 0.05 * jax.random.normal(jax.random.fold_in(_tk, 500 + 19), (1000, 128), jnp.float32)
        tbl_20 = 0.05 * jax.random.normal(jax.random.fold_in(_tk, 500 + 20), (12500, 128), jnp.float32)
        tbl_21 = 0.05 * jax.random.normal(jax.random.fold_in(_tk, 500 + 21), (1250, 128), jnp.float32)
        tbl_22 = 0.05 * jax.random.normal(jax.random.fold_in(_tk, 500 + 22), (12500, 128), jnp.float32)
        tbl_23 = 0.05 * jax.random.normal(jax.random.fold_in(_tk, 500 + 23), (1000, 128), jnp.float32)
        tbl_24 = 0.05 * jax.random.normal(jax.random.fold_in(_tk, 500 + 24), (1000, 128), jnp.float32)
        tbl_25 = 0.05 * jax.random.normal(jax.random.fold_in(_tk, 500 + 25), (1250, 128), jnp.float32)
        tbl_26 = 0.05 * jax.random.normal(jax.random.fold_in(_tk, 500 + 26), (1250, 128), jnp.float32)
        tbl_27 = 0.05 * jax.random.normal(jax.random.fold_in(_tk, 500 + 27), (1250, 128), jnp.float32)
        tbl_28 = 0.05 * jax.random.normal(jax.random.fold_in(_tk, 500 + 28), (1250, 128), jnp.float32)
        tbl_29 = 0.05 * jax.random.normal(jax.random.fold_in(_tk, 500 + 29), (1000, 128), jnp.float32)
        tbl_30 = 0.05 * jax.random.normal(jax.random.fold_in(_tk, 500 + 30), (1250, 128), jnp.float32)
        tbl_31 = 0.05 * jax.random.normal(jax.random.fold_in(_tk, 500 + 31), (1250, 128), jnp.float32)
        tbl_32 = 0.05 * jax.random.normal(jax.random.fold_in(_tk, 500 + 32), (1000, 128), jnp.float32)
        _rk = jax.random.fold_in(_tk, 7)
        r_gnn_feature = -0.00340659 + 1.00146 * jax.random.normal(jax.random.fold_in(_rk, 101), (2048, 128), jnp.float32)
        W_top1 = 0.051031 * jax.random.normal(jax.random.fold_in(_tk, 801), (384, 512), jnp.float32)
        W_top2 = 0.0441942 * jax.random.normal(jax.random.fold_in(_tk, 802), (512, 256), jnp.float32)
        W_top3 = 0.0625 * jax.random.normal(jax.random.fold_in(_tk, 803), (256, 1), jnp.float32)
        b_top1 = jnp.zeros((512,), jnp.float32)
        b_top2 = jnp.zeros((256,), jnp.float32)
        return (r_gnn_feature, ids, tbl_0, tbl_1, tbl_2, tbl_3, tbl_4, tbl_5, tbl_6, tbl_7, tbl_8, tbl_9, tbl_10, tbl_11, tbl_12, tbl_13, tbl_14, tbl_15, tbl_16, tbl_17, tbl_18, tbl_19, tbl_20, tbl_21, tbl_22, tbl_23, tbl_24, tbl_25, tbl_26, tbl_27, tbl_28, tbl_29, tbl_30, tbl_31, tbl_32, W_top1, b_top1, W_top2, b_top2, W_top3)
    r_gnn_feature, ids, tbl_0, tbl_1, tbl_2, tbl_3, tbl_4, tbl_5, tbl_6, tbl_7, tbl_8, tbl_9, tbl_10, tbl_11, tbl_12, tbl_13, tbl_14, tbl_15, tbl_16, tbl_17, tbl_18, tbl_19, tbl_20, tbl_21, tbl_22, tbl_23, tbl_24, tbl_25, tbl_26, tbl_27, tbl_28, tbl_29, tbl_30, tbl_31, tbl_32, W_top1, b_top1, W_top2, b_top2, W_top3 = _rec_inputs()

    def _L0_rec_setup():
        import jax, jax.numpy as jnp
        import numpy as np
        B, F, D, A = (1024, 33, 128, 128)
        key = jax.random.key(seed)
        k1, k2, k3, k4 = jax.random.split(key, 4)
        gnn_feature = jax.random.normal(k1, (B, A), dtype=jnp.float32)
        x = jax.random.normal(k2, (B, F, D), dtype=jnp.float32)
        lim = 1.0 / np.sqrt(D)
        attn_W = jax.random.uniform(k3, (A, D), minval=-lim, maxval=lim, dtype=jnp.float32)
        attn_b = jax.random.uniform(k4, (A,), minval=-lim, maxval=lim, dtype=jnp.float32)
        return {'gnn_feature': gnn_feature, 'x': x, 'attn_W': attn_W, 'attn_b': attn_b}
    _L0_rec_all = _L0_rec_setup()
    _L0_rec_in = {k: v for k, v in _L0_rec_all.items() if k in ('attn_W', 'attn_b')}
    del _L0_rec_all
    return {'r_gnn_feature': r_gnn_feature, 'ids': ids, 'tbl_0': tbl_0, 'tbl_1': tbl_1, 'tbl_2': tbl_2, 'tbl_3': tbl_3, 'tbl_4': tbl_4, 'tbl_5': tbl_5, 'tbl_6': tbl_6, 'tbl_7': tbl_7, 'tbl_8': tbl_8, 'tbl_9': tbl_9, 'tbl_10': tbl_10, 'tbl_11': tbl_11, 'tbl_12': tbl_12, 'tbl_13': tbl_13, 'tbl_14': tbl_14, 'tbl_15': tbl_15, 'tbl_16': tbl_16, 'tbl_17': tbl_17, 'tbl_18': tbl_18, 'tbl_19': tbl_19, 'tbl_20': tbl_20, 'tbl_21': tbl_21, 'tbl_22': tbl_22, 'tbl_23': tbl_23, 'tbl_24': tbl_24, 'tbl_25': tbl_25, 'tbl_26': tbl_26, 'tbl_27': tbl_27, 'tbl_28': tbl_28, 'tbl_29': tbl_29, 'tbl_30': tbl_30, 'tbl_31': tbl_31, 'tbl_32': tbl_32, 'W_top1': W_top1, 'b_top1': b_top1, 'W_top2': W_top2, 'b_top2': b_top2, 'W_top3': W_top3, 'L0_rec_attn_W': _L0_rec_in['attn_W'], 'L0_rec_attn_b': _L0_rec_in['attn_b']}

def reference(r_gnn_feature, ids, tbl_0, tbl_1, tbl_2, tbl_3, tbl_4, tbl_5, tbl_6, tbl_7, tbl_8, tbl_9, tbl_10, tbl_11, tbl_12, tbl_13, tbl_14, tbl_15, tbl_16, tbl_17, tbl_18, tbl_19, tbl_20, tbl_21, tbl_22, tbl_23, tbl_24, tbl_25, tbl_26, tbl_27, tbl_28, tbl_29, tbl_30, tbl_31, tbl_32, W_top1, b_top1, W_top2, b_top2, W_top3, L0_rec_attn_W, L0_rec_attn_b):
    import jax
    import jax.numpy as jnp

    def _L0_rec_ref(gnn_feature, x, attn_W, attn_b):
        import jax, jax.numpy as jnp
        import numpy as np
        B, F, D, A = (1024, 33, 128, 128)
        num_fields = x.shape[1]
        row, col = np.triu_indices(num_fields, k=1)
        inner = x[:, row] * x[:, col]
        fm = jax.nn.relu(jnp.einsum('bpd,ad->bpa', inner, attn_W) + attn_b)
        scores = jnp.einsum('ba,bpa->bp', gnn_feature, fm)
        attn = jax.nn.softmax(scores, axis=1)
        attn_output = jnp.einsum('bp,bpd->bd', attn, inner) * 100.0
        return jnp.concatenate([gnn_feature, attn_output], axis=1)
    e = jnp.stack([tbl_0[ids[:, 0]], tbl_1[ids[:, 1]], tbl_2[ids[:, 2]], tbl_3[ids[:, 3]], tbl_4[ids[:, 4]], tbl_5[ids[:, 5]], tbl_6[ids[:, 6]], tbl_7[ids[:, 7]], tbl_8[ids[:, 8]], tbl_9[ids[:, 9]], tbl_10[ids[:, 10]], tbl_11[ids[:, 11]], tbl_12[ids[:, 12]], tbl_13[ids[:, 13]], tbl_14[ids[:, 14]], tbl_15[ids[:, 15]], tbl_16[ids[:, 16]], tbl_17[ids[:, 17]], tbl_18[ids[:, 18]], tbl_19[ids[:, 19]], tbl_20[ids[:, 20]], tbl_21[ids[:, 21]], tbl_22[ids[:, 22]], tbl_23[ids[:, 23]], tbl_24[ids[:, 24]], tbl_25[ids[:, 25]], tbl_26[ids[:, 26]], tbl_27[ids[:, 27]], tbl_28[ids[:, 28]], tbl_29[ids[:, 29]], tbl_30[ids[:, 30]], tbl_31[ids[:, 31]], tbl_32[ids[:, 32]]], axis=1)
    z = _L0_rec_ref(r_gnn_feature, e, L0_rec_attn_W, L0_rec_attn_b)
    z = z.reshape(z.shape[0], -1)
    h = jnp.concatenate([z, r_gnn_feature], axis=1)
    h = jnp.maximum(h @ W_top1 + b_top1, 0.0)
    h = jnp.maximum(h @ W_top2 + b_top2, 0.0)
    y = h @ W_top3
    return y

_drawn_inputs = setup_inputs


def setup_inputs(seed=0):
    import zlib

    import numpy as np

    out = dict(_drawn_inputs(seed))
    spreads = {'b_top1': (0.0, 0.456), 'b_top2': (0.0, 0.1)}
    factors = {'tbl_0': 8.0,
     'tbl_1': 8.0,
     'tbl_2': 8.0,
     'tbl_3': 8.0,
     'tbl_4': 8.0,
     'tbl_5': 8.0,
     'tbl_6': 8.0,
     'tbl_7': 8.0,
     'tbl_8': 8.0,
     'tbl_9': 8.0,
     'tbl_10': 8.0,
     'tbl_11': 8.0,
     'tbl_12': 8.0,
     'tbl_13': 8.0,
     'tbl_14': 8.0,
     'tbl_15': 8.0,
     'tbl_16': 8.0,
     'tbl_17': 8.0,
     'tbl_18': 8.0,
     'tbl_19': 8.0,
     'tbl_20': 8.0,
     'tbl_21': 8.0,
     'tbl_22': 8.0,
     'tbl_23': 8.0,
     'tbl_24': 8.0,
     'tbl_25': 8.0,
     'tbl_26': 8.0,
     'tbl_27': 8.0,
     'tbl_28': 8.0,
     'tbl_29': 8.0,
     'tbl_30': 8.0,
     'tbl_31': 8.0,
     'tbl_32': 8.0,
     'L0_rec_attn_W': 8.0,
     'L0_rec_attn_b': 8.0}
    for name, (base, spread) in spreads.items():
        noise = np.random.default_rng([zlib.crc32(name.encode()), seed]).standard_normal(out[name].shape)
        drawn = base * np.exp(spread * noise) if base else spread * noise
        out[name] = jnp.asarray(drawn.astype(out[name].dtype))
    for name, factor in factors.items():
        out[name] = (out[name] * factor).astype(out[name].dtype)
    return out
```

```python
from contextlib import ExitStack

import concourse.bass as bass
from concourse import mybir

F32 = mybir.dt.float32
BF16 = mybir.dt.bfloat16
I32 = mybir.dt.int32
ALU = mybir.AluOpType
ACT = mybir.ActivationFunctionType
AX = mybir.AxisListType

P = 128
B, F, D = 2048, 33, 128
TILE = P
TILES = B // TILE
Q = 4
QCOLS = P // Q
STEPS = QCOLS
R = 4
CHUNKS = STEPS // R
ALL_CHUNKS = TILES * CHUNKS
TURN_AHEAD = CHUNKS // 2
MIX_BEHIND = 2 * CHUNKS - TURN_AHEAD
SHIFTS = (F - 1) // 2
FX = F + SHIFTS
FM = F - 1
PAIRS = F * SHIFTS
HALF = PAIRS // 2
STEP_COLS = Q * PAIRS
BLOCK_COLS = 352
BANK = 512
WAVES = STEP_COLS // (2 * BLOCK_COLS)
PARTS = [(0, 11), (11, 22), (22, 32), (32, 33)]
H1, H2 = 512, 256
BLOCK = 512
BLOCKS = B // BLOCK
TOWER = H1 // P + H2 // P + 1
CONSTANTS = 4
WEIGHTS = 8
assert WAVES * 2 * BLOCK_COLS == STEP_COLS and BLOCK_COLS <= BANK and HALF <= BANK
assert R * FM == P and Q * P == BANK


def positive(engine, semaphore, count):
    if type(count) is not int or count > 0:
        engine.wait_ge(semaphore, count)


def all_tiles(engine, tile):
    tile(0, 0, mixes=(False, False))
    tile(1, 1, mixes=(False, True))
    with engine.Fori(2, TILES - 3, 2) as t:
        tile(t, 0)
        tile(t + 1, 1)
    tile(TILES - 2, 0)
    tile(TILES - 1, 1, turns=(True, False))


def build(nc, gnn, ids, tables, w1, b1, w2, b2, w3, attn_w, attn_b, y):
    x_dram = nc.dram_tensor("x_scratch", (TILES, TILE, FM, D), F32, kind="Internal").ap()
    x_last_dram = nc.dram_tensor("x_last_scratch", (TILES, TILE, D), F32, kind="Internal").ap()
    w_dram = nc.dram_tensor("weights_scratch", (TILES, TILE, FM, FM), F32, kind="Internal").ap()

    with ExitStack() as ctx:
        def sb(name, shape, dt=F32):
            return ctx.enter_context(nc.sbuf_tensor(name, shape, dt))

        def psum(name, shape, dt=F32):
            return ctx.enter_context(nc.psum_tensor(name, shape, dt))

        def sem(name):
            return ctx.enter_context(nc.semaphore(name))

        ident = sb("ident", [P, P])
        onehot = sb("onehot", [P, 2 * QCOLS])
        zeros = sb("zeros", [P, HALF], BF16)
        attn_wt = sb("attn_wt", [P, P])
        attn_bias = sb("attn_bias", [P, 1])
        w1_sb = sb("w1_sb", [P, 3, H1])
        w1_gnn = sb("w1_gnn", [P, H1])
        w2_sb = sb("w2_sb", [P, H1 // P, H2])
        w3_sb = sb("w3_sb", [P, H2 // P])
        b1_sb = sb("b1_sb", [P, H1 // P])
        b2_sb = sb("b2_sb", [P, H2 // P])
        gt = sb("gt", [P, B])
        ids_sb = sb("ids_sb", [P, F], I32)
        x_b = sb("x_b", [P, F, D])
        x_turn = [sb(f"x_turn{i}", [P, Q, D]) for i in range(2)]
        x_turn_last = [sb(f"x_turn_last{i}", [Q * R, D]) for i in range(2)]
        x_mix = [sb(f"x_mix{i}", [P, Q, D]) for i in range(2)]
        xt = sb("xt", [P, 2, TILE, FX])
        products = [sb(f"products{i}", [P, STEP_COLS]) for i in range(2)]
        hidden = [sb(f"hidden{i}", [P, STEP_COLS]) for i in range(2)]
        g_col = [sb(f"g_col{i}", [P, Q, QCOLS]) for i in range(2)]
        row_max = sb("row_max", [P, 1])
        neg_max = sb("neg_max", [P, 1])
        row_sum = sb("row_sum", [P, 1])
        inv_sum = sb("inv_sum", [P, 1])
        inv_sum100 = sb("inv_sum100", [P, 1])
        skewed = sb("skewed", [P, F * (FX + 1)])
        folded = sb("folded", [P, FM, FM])
        w_rows = sb("w_rows", [P, 2, Q * CHUNKS, P])
        mixed = [sb(f"mixed{i}", [P, Q, R, FM]) for i in range(2)]
        ao = sb("ao", [P, B])
        y_row = sb("y_row", [1, B])
        g_rows = hidden[0][:, 0:B].rearrange("p (t a) -> p t a", a=D)
        attn_w_rows = hidden[1][:, 0:D]
        h1 = products[1][:, 0:H1 // P * BLOCK].rearrange("p (c n) -> p c n", n=BLOCK)
        h2 = products[0][:, 0:H2 // P * BLOCK].rearrange("p (c n) -> p c n", n=BLOCK)

        raw = psum("raw", [P, 4, BANK])
        mix_bank = psum("mix_bank", [P, BANK])
        turn_bank = psum("turn_bank", [P, BANK])
        scores = psum("scores", [P, 2, BANK])

        constants = sem("constants")
        weights_in = sem("weights_in")
        onehot_made = sem("onehot_made")
        start_turned = sem("start_turned")
        start_kept = sem("start_kept")
        w1_added = sem("w1_added")
        ids_in = sem("ids_in")
        part_free = sem("part_free")
        gathered = [sem(f"gathered{i}") for i in range(len(PARTS))]
        x_stored = [sem(f"x_stored{i}") for i in range(len(PARTS))]
        turn_loaded = [sem(f"turn_loaded{i}") for i in range(2)]
        mix_loaded = [sem(f"mix_loaded{i}") for i in range(2)]
        mix_loads = sem("mix_loads")
        turned = sem("turned")
        last_turns = sem("last_turns")
        kept = sem("kept")
        products_ready = sem("products_ready")
        raw_ready = sem("raw_ready")
        hidden_ready = sem("hidden_ready")
        g_ready = sem("g_ready")
        scored = sem("scored")
        max_found = sem("max_found")
        max_ready = sem("max_ready")
        exp_ready = sem("exp_ready")
        fold_step = sem("fold_step")
        folded_ready = sem("folded_ready")
        w_stored = sem("w_stored")
        w_loaded = sem("w_loaded")
        mix_ready = sem("mix_ready")
        mix_taken = sem("mix_taken")
        ao_ready = sem("ao_ready")
        tower_ready = sem("tower_ready")
        tower_taken = sem("tower_taken")
        y_stored = sem("y_stored")

        skew_write = skewed[:, 0:F * (FX + 1)].rearrange("p (i w) -> p w i", w=FX + 1)
        skew_read = skewed[:, 0:F * FX].rearrange("p (i w) -> p i w", w=FX)
        START = 1 + TILES

        block = ctx.enter_context(nc.Block())

        @block.sync
        def _(sp):
            def next_ids(t):
                sp.dma_start(ids_sb[:], ids[bass.ds(t * TILE, TILE), :]).then_inc(ids_in, 16)

            def store_x(t):
                for part, (lo, hi) in enumerate(PARTS):
                    sp.wait_ge(gathered[part], 16 * (hi - lo) * (t + 1))
                    if hi <= FM:
                        sp.dma_start(x_dram[bass.ds(t, 1), :, lo:hi, :].rearrange("one b f d -> (one b) f d"),
                                     x_b[:, lo:hi, :]).then_inc(x_stored[part], 16)
                    else:
                        sp.dma_start(x_last_dram[bass.ds(t, 1)].rearrange("one b d -> (one b) d"),
                                     x_b[:, FM, :]).then_inc(x_stored[part], 16)

            def chunk_rows(t, c):
                return x_dram[bass.ds(t, 1)].rearrange(
                    "one (q c r) f d -> (one c) (r f) q d", q=Q, r=R)[bass.ds(c, 1)].rearrange(
                    "one p q d -> (one p) q d")

            def load_turn(v, t, c, k):
                positive(sp, turned, 2 * (v - 1))
                sp.dma_start(x_turn[k][:], chunk_rows(t, c)).then_inc(turn_loaded[k], 16)
                sp.dma_start(x_turn_last[k][:], x_last_dram[bass.ds(t, 1)].rearrange(
                    "one (q c r) d -> (one c) q r d", q=Q, r=R)[bass.ds(c, 1)].rearrange(
                    "one q r d -> (one q) r d")).then_inc(turn_loaded[k], 16)

            def load_mix(u, t, c, k):
                sp.wait_ge(mix_ready, u + 1)
                sp.sem_inc(mix_loads, 1)
                sp.dma_start(x_mix[k][:], chunk_rows(t, c)).then_inc(mix_loaded[k], 16)

            def turn_weights(t, parity):
                sp.wait_ge(folded_ready, t + 1)
                sp.dma_start(w_dram[bass.ds(t, 1)].rearrange("one b i k -> (one b) (i k)"),
                             folded[:].rearrange("p i k -> p (i k)")).then_inc(w_stored, 16)
                sp.wait_ge(w_stored, 16 * (t + 1))
                sp.wait_ge(mix_ready, 2 + CHUNKS * max(t - 1, 0) if type(t) is int else 2 + CHUNKS * (t - 1))
                for r in range(R):
                    sp.dma_start(w_rows[FM * r:FM * (r + 1), parity, :, FM * r:FM * (r + 1)],
                                 w_dram[bass.ds(t, 1)].rearrange("one (qc r) i k -> r i (one qc) k", r=R)[r]
                                 ).then_inc(w_loaded, 16)

            sp.dma_start(ids_sb[:], ids[0:TILE, :]).then_inc(ids_in, 16)
            sp.dma_start(attn_w_rows, attn_w).then_inc(weights_in, 16)
            sp.dma_start(g_rows, gnn.rearrange("(t p) a -> p t a", p=P)).then_inc(weights_in, 16)
            sp.dma_start(attn_bias[:], attn_b.rearrange("(p one) -> p one", one=1)).then_inc(weights_in, 16)
            sp.dma_start(w1_sb[:], w1.rearrange("(c p) n -> p c n", p=P)).then_inc(weights_in, 16)
            sp.dma_start(w2_sb[:], w2.rearrange("(c p) n -> p c n", p=P)).then_inc(weights_in, 16)
            with nc.allow_non_contiguous_dma(reason="biases and w3, one column per 128 values"):
                sp.dma_start(w3_sb[:], w3.rearrange("(c p) one -> p (c one)", p=P)).then_inc(weights_in, 16)
                sp.dma_start(b1_sb[:], b1.rearrange("(c p) -> p c", p=P)).then_inc(weights_in, 16)
                sp.dma_start(b2_sb[:], b2.rearrange("(c p) -> p c", p=P)).then_inc(weights_in, 16)
            store_x(0)
            next_ids(1)
            for part in range(len(PARTS)):
                sp.wait_ge(x_stored[part], 16)
            for v in range(TURN_AHEAD + 2):
                load_turn(v, 0, v, v % 2)
            sp.wait_ge(constants, CONSTANTS)

            def tile(t, parity, mixes=(True, True), turns=(True, True)):
                if turns[1]:
                    store_x(t + 1)
                    if type(t) is not int or t + 2 < TILES:
                        next_ids(t + 2)
                for k in range(2):
                    n = CHUNKS * t + k
                    load_turn(n + TURN_AHEAD + 2, t, k + TURN_AHEAD + 2, k)
                    if mixes[0]:
                        load_mix(n + 2 - MIX_BEHIND, t - 2, k + 2 + TURN_AHEAD, k)
                if type(t) is not int or t > 0:
                    turn_weights(t - 1, 1 - parity)
                if turns[1] or mixes[1]:
                    with sp.Fori(2, CHUNKS - 1, 2) as c:
                        if turns[1]:
                            for part in range(len(PARTS)):
                                sp.wait_ge(x_stored[part], 16 * (t + 2))
                        for k in range(2):
                            n = CHUNKS * t + c + k
                            if turns[1]:
                                load_turn(n + TURN_AHEAD + 2, t + 1, c + k + 2 + TURN_AHEAD - CHUNKS, k)
                            if mixes[1]:
                                load_mix(n + 2 - MIX_BEHIND, t - 1, c + k + 2 - TURN_AHEAD, k)

            all_tiles(sp, tile)
            for c in range(2 + TURN_AHEAD, CHUNKS):
                load_mix(CHUNKS * (TILES - 2) + c, TILES - 2, c, c % 2)
            turn_weights(TILES - 1, 1)
            for c in range(CHUNKS):
                load_mix(CHUNKS * (TILES - 1) + c, TILES - 1, c, c % 2)
            sp.wait_ge(tower_taken, BLOCKS * TOWER)
            sp.dma_start(y.rearrange("b one -> one b"), y_row[:]).then_inc(y_stored, 16)
            sp.wait_ge(y_stored, 16)

        @block.gpsimd
        def _(pool):
            def gather(f, part):
                pool.indirect_dma_start(x_b[:, f, :], None, tables[f],
                                        bass.IndirectOffsetOnAxis(ap=ids_sb[:, f:f + 1], axis=0)
                                        ).then_inc(gathered[part], 16)

            pool.memset(ident[:], 0.0).then_inc(constants, 1)
            pool.wait_ge(constants, 1)
            pool.affine_select(out=ident[:], in_=ident[:], compare_op=ALU.not_equal, fill=1.0, base=0,
                               pattern=[[-1, P]], channel_multiplier=1).then_inc(constants, 1)
            pool.wait_ge(ids_in, 16)
            for part, (lo, hi) in enumerate(PARTS):
                for f in range(lo, hi):
                    gather(f, part)
            pool.memset(skewed[:], 0.0).then_inc(constants, 1)
            pool.memset(w_rows[:], 0.0).then_inc(constants, 1)
            with pool.Fori(1, TILES) as t:
                for part, (lo, hi) in enumerate(PARTS):
                    pool.wait_ge(x_stored[part], 16 * t)
                    pool.wait_ge(ids_in, 16 * (t + 1))
                    pool.sem_inc(part_free, 1)
                    for f in range(lo, hi):
                        gather(f, part)

        @block.scalar
        def _(act):
            act.sem_inc(hidden_ready, 2)

            def relu(s, parity):
                act.wait_ge(scored, s + 1)
                for w in range(WAVES):
                    pair = (WAVES * parity + w) % 2
                    act.wait_ge(raw_ready, WAVES * (s + 2) + w + 1)
                    act.activation(
                        hidden[parity][:, 2 * BLOCK_COLS * w:2 * BLOCK_COLS * (w + 1)
                                       ].rearrange("p (c n) -> p c n", c=2),
                        raw[:, 2 * pair:2 * pair + 2, 0:BLOCK_COLS], ACT.Relu, bias=attn_bias[:, 0:1]
                    ).then_inc(hidden_ready, 1)

            def exp(t):
                positive(act, folded_ready, t)
                act.wait_ge(max_ready, t + 1)
                act.activation(skew_write[:, 1:SHIFTS + 1, :].rearrange("p (h s) i -> p h s i", h=2),
                               scores[:, :, 0:HALF].rearrange("p h (s i) -> p h s i", i=F), ACT.Exp,
                               bias=neg_max[:, 0:1], accum_out=row_sum[:, 0:1]).then_inc(exp_ready, 1)

            def chunk_of_xt(parity, c):
                return xt[:, parity].rearrange("p (q c r) f -> p c q r f", q=Q, r=R)[:, bass.ds(c, 1)].rearrange(
                    "p one q r f -> p (one q) r f")

            def keep_turned(v, parity, c, again):
                if again:
                    act.wait_ge(mix_taken, v - 2 * CHUNKS + 2)
                act.wait_ge(turned, 2 * v + 1)
                at = chunk_of_xt(parity, c)
                fields = turn_bank[:].rearrange("p (q r f) -> p q r f", q=Q, f=FM)
                act.activation(at[:, :, :, F:FX], fields[:, :, :, 0:SHIFTS], ACT.Copy)
                act.activation(at[:, :, :, 0:FM], fields, ACT.Copy).then_inc(kept, 1)

            def keep_last(v, parity, c):
                act.wait_ge(turned, 2 * v + 2)
                act.activation(chunk_of_xt(parity, c)[:, :, :, FM],
                               turn_bank[:, 0:Q * R].rearrange("p (q r) -> p q r", q=Q), ACT.Copy
                               ).then_inc(kept, 1)

            def two_chunks(t, parity, c, half, mixes, turns, softmax=False):
                for k in range(2):
                    n = CHUNKS * t + c + k
                    to = (n + TURN_AHEAD, (parity, 1 - parity)[half], c + k + (TURN_AHEAD, TURN_AHEAD - CHUNKS)[half])
                    for j in range(R):
                        relu(R * n + j, j % 2)
                        if softmax and k == 0 and j == 0:
                            exp(t - 1)
                        if turns and j == 2:
                            keep_turned(*to, again=mixes)
                        if turns and j == 3:
                            keep_last(*to)

            def tile(t, parity, mixes=(True, True), turns=(True, True)):
                two_chunks(t, parity, 0, 0, mixes[0], turns[0], softmax=type(t) is not int or t > 0)
                two_chunks(t, parity, 2, 0, mixes[0], turns[0])
                with act.Fori(TURN_AHEAD, CHUNKS - 1, 2) as c:
                    two_chunks(t, parity, c, 1, mixes[1], turns[1])

            act.wait_ge(weights_in, 16 * WEIGHTS)
            for v in range(TURN_AHEAD):
                keep_turned(v, 0, v, again=False)
                keep_last(v, 0, v)
            act.wait_ge(start_kept, START)
            act.wait_ge(constants, CONSTANTS)
            all_tiles(act, tile)
            exp(TILES - 1)

            def tower(blk, at):
                k = 0
                for c in range(H1 // P):
                    act.wait_ge(tower_ready, at + k + 1)
                    act.activation(h1[:, c, :], raw[:, (at + k) % 4, :], ACT.Relu, bias=b1_sb[:, c:c + 1]
                                   ).then_inc(tower_taken, 1)
                    k += 1
                for c in range(H2 // P):
                    act.wait_ge(tower_ready, at + k + 1)
                    act.activation(h2[:, c, :], raw[:, (at + k) % 4, :], ACT.Relu, bias=b2_sb[:, c:c + 1]
                                   ).then_inc(tower_taken, 1)
                    k += 1
                act.wait_ge(tower_ready, at + k + 1)
                act.activation(y_row[0:1, blk * BLOCK:(blk + 1) * BLOCK], raw[0:1, (at + k) % 4, :], ACT.Copy
                               ).then_inc(tower_taken, 1)

            for blk in range(BLOCKS):
                tower(blk, TOWER * blk)

        @block.vector
        def _(dve):
            dve.sem_inc(mix_taken, 1)
            dve.sem_inc(ao_ready, 2)
            dve.memset(onehot[:], 0.0).then_inc(onehot_made, 1)
            dve.memset(zeros[:], 0.0).then_inc(onehot_made, 1)
            dve.wait_ge(onehot_made, 1)
            dve.memset(onehot[:, QCOLS:QCOLS + 1], 1.0).then_inc(onehot_made, 1)
            for n in range(START):
                dve.wait_ge(start_turned, n + 1)
                dst = attn_wt[:] if n == 0 else gt[:, (n - 1) * TILE:n * TILE]
                dve.tensor_copy(dst, (mix_bank, turn_bank)[n % 2][:, 0:TILE]).then_inc(start_kept, 1)
            dve.wait_ge(weights_in, 16 * WEIGHTS)
            dve.tensor_tensor(w1_gnn[:], w1_sb[:, 0, :], w1_sb[:, 2, :], ALU.add).then_inc(w1_added, 1)
            dve.wait_ge(onehot_made, 3)
            dve.wait_ge(start_kept, START)

            def multiply(s, m, tile_parity, parity):
                dve.wait_ge(raw_ready, WAVES * (s + 1))
                row = xt[:, tile_parity, bass.ds(m, 1), 0:F]
                at, step_q = row.offset, QCOLS * FX
                left = bass.AP(row.tensor, at, [row.ap[0], [step_q, Q], [0, SHIFTS], [1, F]])
                right = bass.AP(row.tensor, at + 1, [row.ap[0], [step_q, Q], [1, SHIFTS], [1, F]])
                dve.tensor_tensor(products[parity][:].rearrange("p (q s i) -> p q s i", q=Q, i=F),
                                  left, right, ALU.mult).then_inc(products_ready, 1)

            def place_g(s, t, m, parity):
                dve.wait_ge(scored, s + 1)
                g4 = gt[:, bass.ds(t * TILE + m, 1)]
                g4 = bass.AP(g4.tensor, g4.offset, [g4.ap[0], [QCOLS, Q], [0, QCOLS]])
                hot = onehot[:, bass.ds(QCOLS - m, QCOLS)]
                hot = bass.AP(hot.tensor, hot.offset, [hot.ap[0], [0, Q], [1, QCOLS]])
                dve.tensor_tensor(g_col[parity][:], g4, hot, ALU.mult).then_inc(g_ready, 1)

            def find_max(t):
                dve.wait_ge(scored, 2 + STEPS * (t + 1))
                positive(dve, exp_ready, t)
                dve.tensor_reduce(row_max[:], scores[:, :, 0:HALF], AX.XY, ALU.max).then_inc(max_found, 1)
                dve.wait_ge(max_found, t + 1)
                dve.tensor_scalar(neg_max[:], row_max[:], -1.0, None, ALU.mult).then_inc(max_ready, 1)

            def fold(t):
                dve.wait_ge(exp_ready, t + 1)
                dve.reciprocal(inv_sum[:], row_sum[:]).then_inc(fold_step, 1)
                dve.wait_ge(fold_step, 3 * t + 1)
                dve.tensor_scalar(inv_sum100[:], inv_sum[:], 100.0, None, ALU.mult).then_inc(fold_step, 1)
                positive(dve, w_stored, 16 * t)
                dve.wait_ge(fold_step, 3 * t + 2)
                dve.tensor_scalar(folded[:], skew_read[:, 0:FM, 1:F], inv_sum100[:, 0:1], None, ALU.mult
                                  ).then_inc(fold_step, 1)
                dve.wait_ge(fold_step, 3 * t + 3)
                wrapped = skew_read[:, F - SHIFTS:F, F:FX].rearrange("p k i -> p i k")
                dve.scalar_tensor_tensor(out=folded[:, 0:SHIFTS, FM - SHIFTS:FM], in0=wrapped,
                                         scalar=inv_sum100[:, 0:1], in1=folded[:, 0:SHIFTS, FM - SHIFTS:FM],
                                         op0=ALU.mult, op1=ALU.add).then_inc(folded_ready, 1)

            def finish_mix(u, t, parity, c, k):
                dve.wait_ge(mix_ready, u + 3)
                dve.wait_ge(ao_ready, u + 1)
                right = xt[:, parity].rearrange("p (q c r) f -> p c q r f", q=Q, r=R)[:, bass.ds(c, 1)].rearrange(
                    "p one q r f -> p (one q) r f")[:, :, :, 1:F]
                dve.tensor_tensor(mixed[k][:], mix_bank[:].rearrange("p (q r f) -> p q r f", q=Q, f=FM),
                                  right, ALU.mult).then_inc(mix_taken, 1)
                dve.wait_ge(mix_taken, u + 2)
                out = ao[:, bass.ds(t * TILE + R * c, 1)]
                out = bass.AP(out.tensor, out.offset, [out.ap[0], [QCOLS, Q], [1, R]])
                dve.tensor_reduce(out, mixed[k][:], AX.X, ALU.add).then_inc(ao_ready, 1)

            def two_chunks(t, parity, c, half, mixes, softmax=False):
                for k in range(2):
                    n = CHUNKS * t + c + k
                    dve.wait_ge(kept, 2 * (n + 1))
                    for j in range(R):
                        m = R * (c + k) + j
                        multiply(STEPS * t + m, m, parity, j % 2)
                        place_g(STEPS * t + m, t, m, j % 2)
                        if softmax and k == 0 and j == 1:
                            find_max(t - 1)
                        if mixes and j == 2:
                            finish_mix(n - MIX_BEHIND, t - 2 + half, (parity, 1 - parity)[half],
                                       c + k + (TURN_AHEAD, -TURN_AHEAD)[half], k)

            def tile(t, parity, mixes=(True, True), turns=(True, True)):
                later = type(t) is not int or t > 0
                two_chunks(t, parity, 0, 0, mixes[0], softmax=later)
                if later:
                    fold(t - 1)
                two_chunks(t, parity, 2, 0, mixes[0])
                with dve.Fori(TURN_AHEAD, CHUNKS - 1, 2) as c:
                    two_chunks(t, parity, c, 1, mixes[1])

            all_tiles(dve, tile)
            find_max(TILES - 1)
            for c in range(TURN_AHEAD, CHUNKS):
                finish_mix(CHUNKS * (TILES - 2) + c, TILES - 2, 0, c, c % 2)
            fold(TILES - 1)
            for c in range(CHUNKS):
                finish_mix(CHUNKS * (TILES - 1) + c, TILES - 1, 1, c, c % 2)

        @block.tensor
        def _(pe):
            pe.sem_inc(raw_ready, 2 * WAVES)
            pe.sem_inc(mix_ready, 2)
            pe.sem_inc(scored, 2)

            def turn(v, pairs, k):
                pe.wait_ge(turn_loaded[k], 32 * (pairs + 1))
                positive(pe, kept, 2 * v)
                for q in range(Q):
                    last = pe.transpose(turn_bank[:, P * q:P * (q + 1)], x_turn[k][:, q, :], ident[:])
                last.then_inc(turned, 1)

            def turn_last(v, k):
                pe.wait_ge(kept, 2 * v + 1)
                pe.sem_inc(last_turns, 1)
                pe.transpose(turn_bank[:, 0:Q * R], x_turn_last[k][:], ident[0:Q * R, 0:Q * R]
                             ).then_inc(turned, 1)

            def mix(u, pairs, t, parity, c, k):
                pe.wait_ge(w_loaded, 16 * R * (t + 1))
                pe.wait_ge(mix_loaded[k], 16 * (pairs + 1))
                pe.wait_ge(mix_taken, u + 1)
                for q in range(Q):
                    last = pe.matmul(mix_bank[:, P * q:P * (q + 1)], x_mix[k][:, q, :],
                                     w_rows[:, parity, bass.ds(CHUNKS * q + c, 1), :].rearrange(
                                         "p one n -> p (one n)"), start=True, stop=True)
                last.then_inc(mix_ready, 1)

            def hide(s, parity):
                pe.wait_ge(products_ready, s + 1)
                for w in range(WAVES):
                    pair = (WAVES * parity + w) % 2
                    pe.wait_ge(hidden_ready, WAVES * s + w + 1)
                    for c in range(2):
                        at = (2 * w + c) * BLOCK_COLS
                        last = pe.matmul(raw[:, 2 * pair + c, 0:BLOCK_COLS], attn_wt[:],
                                         products[parity][:, at:at + BLOCK_COLS], start=True, stop=True)
                    last.then_inc(raw_ready, 1)

            def score(s, parity):
                pe.wait_ge(g_ready, s + 1)
                pe.wait_ge(hidden_ready, 2 + WAVES * (s + 1))
                for h in range(2):
                    for q in range(Q):
                        at = q * PAIRS + h * HALF
                        last = pe.matmul(scores[QCOLS * q:QCOLS * (q + 1), h, 0:HALF], g_col[parity][:, q, :],
                                         hidden[parity][:, at:at + HALF], start=False, stop=False,
                                         skip_group_check=True)
                last.then_inc(scored, 1)

            def clear_scores(t):
                positive(pe, exp_ready, t)
                for h in range(2):
                    pe.matmul(scores[:, h, 0:HALF], zeros[:, 0:P], zeros[:], start=True, stop=False,
                              skip_group_check=True)

            def two_chunks(t, parity, c, pairs, half, mixes, turns, head=False):
                for k in range(2):
                    n = CHUNKS * t + c + k
                    for j in range(R):
                        hide(R * n + j, j % 2)
                        if head and k == 0 and j == 1:
                            clear_scores(t)
                        if not (head and type(t) is int and t == 0 and k == 0 and j == 0):
                            score(R * n + j - 1, (j + 1) % 2)
                        if mixes and j == 0:
                            mix(n - MIX_BEHIND, pairs - MIX_BEHIND // 2, t - 2 + half, (parity, 1 - parity)[half],
                                c + k + (TURN_AHEAD, -TURN_AHEAD)[half], k)
                        if turns and j == 1:
                            turn(n + TURN_AHEAD, pairs + TURN_AHEAD // 2, k)
                        if turns and j == 3:
                            turn_last(n + TURN_AHEAD, k)

            def tile(t, parity, mixes=(True, True), turns=(True, True)):
                pairs = CHUNKS // 2 * t
                two_chunks(t, parity, 0, pairs, 0, mixes[0], turns[0], head=True)
                two_chunks(t, parity, 2, pairs + 1, 0, mixes[0], turns[0])
                with pe.Fori(TURN_AHEAD // 2, CHUNKS // 2) as pair:
                    two_chunks(t, parity, 2 * pair, pairs + pair, 1, mixes[1], turns[1])

            pe.wait_ge(constants, 2)
            pe.wait_ge(weights_in, 16 * WEIGHTS)
            for n in range(START):
                if n >= 2:
                    pe.wait_ge(start_kept, n - 1)
                pe.transpose((mix_bank, turn_bank)[n % 2][:, 0:TILE],
                             attn_w_rows if n == 0 else g_rows[:, n - 1, :], ident[:]).then_inc(start_turned, 1)
            pe.wait_ge(start_kept, START)
            for v in range(TURN_AHEAD):
                turn(v, v // 2, v % 2)
                turn_last(v, v % 2)
            pe.wait_ge(onehot_made, 3)
            all_tiles(pe, tile)
            score(STEPS * TILES - 1, 1)
            for c in range(TURN_AHEAD, CHUNKS):
                u = CHUNKS * (TILES - 2) + c
                mix(u, u // 2, TILES - 2, 0, c, c % 2)

            def tower(blk, at):
                cols = slice(blk * BLOCK, (blk + 1) * BLOCK)
                k = 0
                for c in range(H1 // P):
                    positive(pe, tower_taken, at + k - 3)
                    pe.matmul(raw[:, (at + k) % 4, :], w1_gnn[:, c * P:(c + 1) * P], gt[:, cols],
                              start=True, stop=False)
                    pe.matmul(raw[:, (at + k) % 4, :], w1_sb[:, 1, c * P:(c + 1) * P], ao[:, cols],
                              start=False, stop=True).then_inc(tower_ready, 1)
                    k += 1
                for c in range(H2 // P):
                    pe.wait_ge(tower_taken, at + H1 // P)
                    for j in range(H1 // P):
                        last = pe.matmul(raw[:, (at + k) % 4, :], w2_sb[:, j, c * P:(c + 1) * P], h1[:, j, :],
                                         start=(j == 0), stop=(j == H1 // P - 1))
                    last.then_inc(tower_ready, 1)
                    k += 1
                pe.wait_ge(tower_taken, at + (H1 + H2) // P)
                for j in range(H2 // P):
                    last = pe.matmul(raw[0:1, (at + k) % 4, :], w3_sb[:, j:j + 1], h2[:, j, :],
                                     start=(j == 0), stop=(j == H2 // P - 1))
                last.then_inc(tower_ready, 1)

            pe.wait_ge(w1_added, 1)
            pe.wait_ge(ao_ready, 2 + CHUNKS * (TILES - 1) - CHUNKS // 2)
            for blk in range(BLOCKS - 1):
                tower(blk, TOWER * blk)
            for c in range(CHUNKS):
                u = CHUNKS * (TILES - 1) + c
                mix(u, u // 2, TILES - 1, 1, c, c % 2)
            pe.wait_ge(ao_ready, 2 + ALL_CHUNKS)
            tower(BLOCKS - 1, TOWER * (BLOCKS - 1))


def kernel(**inputs):
    import numpy as np
    import concourse.bacc as bacc
    from concourse.bass_utils import run_bass_kernel_spmd

    nc = bacc.Bacc("TRN2", target_bir_lowering=False, num_devices=1)
    arrays = {}

    def given(name):
        a = np.ascontiguousarray(inputs[name])
        arrays[f"in_{name}"] = a
        return nc.dram_tensor(f"in_{name}", a.shape, mybir.dt.from_np(a.dtype), kind="ExternalInput").ap()

    gnn, ids = given("r_gnn_feature"), given("ids")
    tables = [given(f"tbl_{f}") for f in range(F)]
    rest = [given(n) for n in ("W_top1", "b_top1", "W_top2", "b_top2", "W_top3", "L0_rec_attn_W", "L0_rec_attn_b")]
    y = nc.dram_tensor("out_y", (B, 1), F32, kind="ExternalOutput").ap()
    build(nc, gnn, ids, tables, *rest, y)
    result = run_bass_kernel_spmd(nc, [arrays], core_ids=[0])
    return result.results[0]["out_y"]
```

```python
from contextlib import ExitStack

import concourse.bass as bass
from concourse import mybir

F32 = mybir.dt.float32
BF16 = mybir.dt.bfloat16
I32 = mybir.dt.int32
ALU = mybir.AluOpType
ACT = mybir.ActivationFunctionType
AX = mybir.AxisListType

P = 128
B, F, D = 2048, 33, 128
TILE = P
TILES = B // TILE
Q = 4
QCOLS = P // Q
STEPS = QCOLS
R = 4
CHUNKS = STEPS // R
ALL_CHUNKS = TILES * CHUNKS
TURN_AHEAD = CHUNKS // 2
MIX_BEHIND = 2 * CHUNKS - TURN_AHEAD
SHIFTS = (F - 1) // 2
FX = F + SHIFTS
FM = F - 1
PAIRS = F * SHIFTS
HALF = PAIRS // 2
STEP_COLS = Q * PAIRS
BLOCK_COLS = 352
BANK = 512
WAVES = STEP_COLS // (2 * BLOCK_COLS)
PARTS = [(0, 14), (14, 28), (28, 32), (32, 33)]
H1, H2 = 512, 256
BLOCK = 512
BLOCKS = B // BLOCK
L1, L2 = H1 // P, H2 // P
FIELD_GROUPS = [(part, f, min(f + Q, hi)) for part, (lo, hi) in enumerate(PARTS) for f in range(lo, hi, Q)]
WEIGHTS = 6
assert WAVES * 2 * BLOCK_COLS == STEP_COLS and BLOCK_COLS <= BANK and HALF <= BANK
assert R * FM == P and Q * P == BANK


def tower_order():
    order = []
    for blk in range(BLOCKS):
        order += [(1, blk, c) for c in range(L1)]
        if blk > 0:
            order.append((3, blk - 1, 0))
        order += [(2, blk, c) for c in range(L2)]
    return order + [(3, BLOCKS - 1, 0)]


TOWER = tower_order()
MIXES_AFTER = {(1, 0, 3): 2, (2, 0, 0): 1, (2, 0, 1): 1,
               (2, 1, 0): 2, (2, 1, 1): 2, (1, 2, 3): 1, (3, 1, 0): 1, (2, 2, 0): 2}
assert sum(MIXES_AFTER.values()) == MIX_BEHIND


def late_mixes(n):
    first = ALL_CHUNKS - MIX_BEHIND + sum(MIXES_AFTER.get(bank, 0) for bank in TOWER[:n])
    return range(first, first + MIXES_AFTER.get(TOWER[n], 0))


def positive(engine, semaphore, count):
    if type(count) is not int or count > 0:
        engine.wait_ge(semaphore, count)


def all_tiles(engine, tile):
    tile(0, 0, mixes=(False, False), turns=(False, True))
    tile(1, 1, mixes=(False, True))
    with engine.Fori(2, TILES - 3, 2) as t:
        tile(t, 0)
        tile(t + 1, 1)
    tile(TILES - 2, 0)
    tile(TILES - 1, 1, turns=(True, False))


def build(nc, gnn, ids, tables, w1, b1, w2, b2, w3, attn_w, attn_b, y):
    x_dram = nc.dram_tensor("x_scratch", (TILES, TILE, FM, D), F32, kind="Internal").ap()
    x_last_dram = nc.dram_tensor("x_last_scratch", (TILES, TILE, D), F32, kind="Internal").ap()
    w_dram = nc.dram_tensor("weights_scratch", (TILES, TILE, FM, FM), F32, kind="Internal").ap()
    l1_dram = nc.dram_tensor("layer1_scratch", (P, BLOCKS * L1 * BLOCK), F32, kind="Internal").ap()

    with ExitStack() as ctx:
        def sb(name, shape, dt=F32):
            return ctx.enter_context(nc.sbuf_tensor(name, shape, dt))

        def psum(name, shape, dt=F32):
            return ctx.enter_context(nc.psum_tensor(name, shape, dt))

        def sem(name):
            return ctx.enter_context(nc.semaphore(name))

        ident = sb("ident", [P, P])
        onehot = sb("onehot", [P, 2 * QCOLS])
        zeros = sb("zeros", [P, HALF], BF16)
        attn_wt = sb("attn_wt", [P, P])
        attn_bias = sb("attn_bias", [P, 1])
        w1_sb = sb("w1_sb", [P, 3, H1])
        w1_gnn = sb("w1_gnn", [P, H1])
        w2_sb = sb("w2_sb", [P, H1 // P, H2])
        w3_sb = sb("w3_sb", [P, H2 // P])
        b1_sb = sb("b1_sb", [P, H1 // P])
        b2_sb = sb("b2_sb", [P, H2 // P])
        gt = sb("gt", [P, B])
        ids_sb = sb("ids_sb", [P, F], I32)
        x_b = sb("x_b", [P, F, D])
        x_turn = [sb(f"x_turn{i}", [P, Q, D]) for i in range(2)]
        x_turn_last = [sb(f"x_turn_last{i}", [Q * R, D]) for i in range(2)]
        x_mix = [sb(f"x_mix{i}", [P, Q, D]) for i in range(2)]
        xt = sb("xt", [P, 2, TILE, FX])
        products = [sb(f"products{i}", [P, STEP_COLS]) for i in range(2)]
        hidden = [sb(f"hidden{i}", [P, STEP_COLS]) for i in range(R)]
        g_col = [sb(f"g_col{i}", [P, Q, QCOLS]) for i in range(R)]
        row_max = sb("row_max", [P, 1])
        neg_max = sb("neg_max", [P, 1])
        row_sum = sb("row_sum", [P, 1])
        inv_sum = sb("inv_sum", [P, 1])
        inv_sum100 = sb("inv_sum100", [P, 1])
        skewed = sb("skewed", [P, F * (FX + 1)])
        folded = sb("folded", [P, FM, FM])
        w_rows = sb("w_rows", [P, 2, Q * CHUNKS, P])
        mixed = [sb(f"mixed{i}", [P, Q, R, FM]) for i in range(2)]
        ao = sb("ao", [P, B])
        g_rows = hidden[0][:, 0:B].rearrange("p (t a) -> p t a", a=D)
        attn_w_rows = hidden[1][:, 0:D]
        y_row = hidden[0][0:1, 0:B]
        h1 = products[1][:, 0:L1 * BLOCK].rearrange("p (c n) -> p c n", n=BLOCK)
        h2 = products[0][:, 0:L2 * BLOCK].rearrange("p (c n) -> p c n", n=BLOCK)
        l1_made = w_rows[:].rearrange("p a qc n -> p (a qc n)")
        x_b_flat = x_b[:].rearrange("p f d -> p (f d)")
        l1_gnn = [x_b_flat[:, 0:L1 * BLOCK], x_b_flat[:, L1 * BLOCK:2 * L1 * BLOCK],
                  hidden[1][:, 0:L1 * BLOCK], hidden[2][:, 0:L1 * BLOCK]]

        raw = psum("raw", [P, 4, BANK])
        mix_bank = psum("mix_bank", [P, BANK])
        turn_bank = psum("turn_bank", [P, BANK])
        scores = psum("scores", [P, 2, BANK])

        constants = sem("constants")
        skewed_zeroed = sem("skewed_zeroed")
        w_rows_zeroed = sem("w_rows_zeroed")
        start_in = sem("start_in")
        weights_in = sem("weights_in")
        onehot_made = sem("onehot_made")
        start_turned = sem("start_turned")
        start_kept = sem("start_kept")
        w1_added = sem("w1_added")
        l1_product = sem("l1_product")
        l1_kept = sem("l1_kept")
        l1_stored = sem("l1_stored")
        l1_loaded = [sem(f"l1_loaded{i}") for i in range(BLOCKS)]
        fields_turned = sem("fields_turned")
        fields_kept = sem("fields_kept")
        ids_in = sem("ids_in")
        part_free = sem("part_free")
        gathered = [sem(f"gathered{i}") for i in range(len(PARTS))]
        x_stored = [sem(f"x_stored{i}") for i in range(len(PARTS))]
        turn_loaded = [sem(f"turn_loaded{i}") for i in range(2)]
        mix_loaded = [sem(f"mix_loaded{i}") for i in range(2)]
        mix_loads = sem("mix_loads")
        turned = sem("turned")
        last_turns = sem("last_turns")
        kept = sem("kept")
        products_ready = sem("products_ready")
        raw_ready = sem("raw_ready")
        hidden_ready = sem("hidden_ready")
        g_ready = sem("g_ready")
        scored = sem("scored")
        max_found = sem("max_found")
        max_ready = sem("max_ready")
        exp_ready = sem("exp_ready")
        fold_step = sem("fold_step")
        folded_ready = sem("folded_ready")
        w_stored = sem("w_stored")
        w_loaded = sem("w_loaded")
        mix_ready = sem("mix_ready")
        mix_taken = sem("mix_taken")
        ao_ready = sem("ao_ready")
        tower_ready = sem("tower_ready")
        l1_summed = sem("l1_summed")
        tower_taken = sem("tower_taken")
        y_stored = sem("y_stored")

        skew_write = skewed[:, 0:F * (FX + 1)].rearrange("p (i w) -> p w i", w=FX + 1)
        skew_read = skewed[:, 0:F * FX].rearrange("p (i w) -> p i w", w=FX)
        START = 1 + TILES

        block = ctx.enter_context(nc.Block())

        @block.sync
        def _(sp):
            def next_ids(t):
                sp.dma_start(ids_sb[:], ids[bass.ds(t * TILE, TILE), :]).then_inc(ids_in, 16)

            def store_x(t):
                for part, (lo, hi) in enumerate(PARTS):
                    sp.wait_ge(gathered[part], 16 * (hi - lo) * (t + 1))
                    if hi <= FM:
                        sp.dma_start(x_dram[bass.ds(t, 1), :, lo:hi, :].rearrange("one b f d -> (one b) f d"),
                                     x_b[:, lo:hi, :]).then_inc(x_stored[part], 16)
                    else:
                        sp.dma_start(x_last_dram[bass.ds(t, 1)].rearrange("one b d -> (one b) d"),
                                     x_b[:, FM, :]).then_inc(x_stored[part], 16)

            def chunk_rows(t, c):
                return x_dram[bass.ds(t, 1)].rearrange(
                    "one (q c r) f d -> (one c) (r f) q d", q=Q, r=R)[bass.ds(c, 1)].rearrange(
                    "one p q d -> (one p) q d")

            def load_turn(v, t, c, k):
                sp.wait_ge(turned, 2 * (v - 1))
                sp.dma_start(x_turn[k][:], chunk_rows(t, c)).then_inc(turn_loaded[k], 16)
                sp.dma_start(x_turn_last[k][:], x_last_dram[bass.ds(t, 1)].rearrange(
                    "one (q c r) d -> (one c) q r d", q=Q, r=R)[bass.ds(c, 1)].rearrange(
                    "one q r d -> (one q) r d")).then_inc(turn_loaded[k], 16)

            def load_mix(u, t, c, k):
                sp.wait_ge(mix_ready, u + 1)
                sp.sem_inc(mix_loads, 1)
                sp.dma_start(x_mix[k][:], chunk_rows(t, c)).then_inc(mix_loaded[k], 16)

            def turn_weights(t, parity):
                sp.wait_ge(folded_ready, t + 1)
                sp.dma_start(w_dram[bass.ds(t, 1)].rearrange("one b i k -> (one b) (i k)"),
                             folded[:].rearrange("p i k -> p (i k)")).then_inc(w_stored, 16)
                sp.wait_ge(w_stored, 16 * (t + 1))
                sp.wait_ge(mix_ready, 2 + CHUNKS * max(t - 1, 0) if type(t) is int else 2 + CHUNKS * (t - 1))
                for r in range(R):
                    sp.dma_start(w_rows[FM * r:FM * (r + 1), parity, :, FM * r:FM * (r + 1)],
                                 w_dram[bass.ds(t, 1)].rearrange("one (qc r) i k -> r i (one qc) k", r=R)[r]
                                 ).then_inc(w_loaded, 16)

            sp.dma_start(ids_sb[:], ids[0:TILE, :]).then_inc(ids_in, 16)
            sp.dma_start(attn_w_rows, attn_w).then_inc(start_in, 16)
            sp.dma_start(g_rows, gnn.rearrange("(t p) a -> p t a", p=P)).then_inc(start_in, 16)
            sp.dma_start(attn_bias[:], attn_b.rearrange("(p one) -> p one", one=1)).then_inc(weights_in, 16)
            sp.dma_start(w1_sb[:], w1.rearrange("(c p) n -> p c n", p=P)).then_inc(weights_in, 16)
            sp.dma_start(w2_sb[:], w2.rearrange("(c p) n -> p c n", p=P)).then_inc(weights_in, 16)
            with nc.allow_non_contiguous_dma(reason="biases and w3, one column per 128 values"):
                sp.dma_start(w3_sb[:], w3.rearrange("(c p) one -> p (c one)", p=P)).then_inc(weights_in, 16)
                sp.dma_start(b1_sb[:], b1.rearrange("(c p) -> p c", p=P)).then_inc(weights_in, 16)
                sp.dma_start(b2_sb[:], b2.rearrange("(c p) -> p c", p=P)).then_inc(weights_in, 16)
            store_x(0)
            next_ids(1)
            sp.wait_ge(l1_kept, BLOCKS * L1)
            sp.dma_start(l1_dram, l1_made).then_inc(l1_stored, 16)

            def load_l1(blk):
                sp.dma_start(l1_gnn[blk], l1_dram[:, L1 * BLOCK * blk:L1 * BLOCK * (blk + 1)]
                             ).then_inc(l1_loaded[blk], 16)

            def tile(t, parity, mixes=(True, True), turns=(True, True)):
                if turns[1]:
                    store_x(t + 1)
                    if type(t) is not int or t + 2 < TILES:
                        next_ids(t + 2)
                else:
                    for part in range(len(PARTS)):
                        sp.wait_ge(x_stored[part], 16 * TILES)
                    load_l1(0)
                    load_l1(1)
                for k in range(2):
                    n = CHUNKS * t + k
                    if turns[0]:
                        load_turn(n + TURN_AHEAD + 2, t, k + TURN_AHEAD + 2, k)
                    if mixes[0]:
                        load_mix(n + 2 - MIX_BEHIND, t - 2, k + 2 + TURN_AHEAD, k)
                if type(t) is int and t == 1:
                    sp.wait_ge(w_rows_zeroed, 1)
                if type(t) is not int or t > 0:
                    turn_weights(t - 1, 1 - parity)
                if turns[1] or mixes[1]:
                    with sp.Fori(2, CHUNKS - 1, 2) as c:
                        if turns[1]:
                            for part in range(len(PARTS)):
                                sp.wait_ge(x_stored[part], 16 * (t + 2))
                        for k in range(2):
                            n = CHUNKS * t + c + k
                            if turns[1]:
                                load_turn(n + TURN_AHEAD + 2, t + 1, c + k + 2 + TURN_AHEAD - CHUNKS, k)
                            if mixes[1]:
                                load_mix(n + 2 - MIX_BEHIND, t - 1, c + k + 2 - TURN_AHEAD, k)

            all_tiles(sp, tile)
            for c in range(2 + TURN_AHEAD, CHUNKS):
                load_mix(CHUNKS * (TILES - 2) + c, TILES - 2, c, c % 2)
            turn_weights(TILES - 1, 1)
            for blk in range(2, BLOCKS):
                load_l1(blk)
            for c in range(CHUNKS):
                load_mix(CHUNKS * (TILES - 1) + c, TILES - 1, c, c % 2)
            sp.wait_ge(tower_taken, len(TOWER))
            sp.dma_start(y.rearrange("b one -> one b"), y_row).then_inc(y_stored, 16)
            sp.wait_ge(y_stored, 16)

        @block.gpsimd
        def _(pool):
            def gather(f, part):
                pool.indirect_dma_start(x_b[:, f, :], None, tables[f],
                                        bass.IndirectOffsetOnAxis(ap=ids_sb[:, f:f + 1], axis=0)
                                        ).then_inc(gathered[part], 16)

            pool.memset(ident[:], 0.0).then_inc(constants, 1)
            pool.wait_ge(constants, 1)
            pool.affine_select(out=ident[:], in_=ident[:], compare_op=ALU.not_equal, fill=1.0, base=0,
                               pattern=[[-1, P]], channel_multiplier=1).then_inc(constants, 1)
            pool.wait_ge(ids_in, 16)
            for part, (lo, hi) in enumerate(PARTS):
                for f in range(lo, hi):
                    gather(f, part)
            pool.memset(skewed[:], 0.0).then_inc(skewed_zeroed, 1)
            pool.wait_ge(l1_stored, 16)
            pool.memset(w_rows[:], 0.0).then_inc(w_rows_zeroed, 1)
            pool.wait_ge(fields_turned, len(FIELD_GROUPS))
            with pool.Fori(1, TILES) as t:
                for part, (lo, hi) in enumerate(PARTS):
                    pool.wait_ge(x_stored[part], 16 * t)
                    pool.wait_ge(ids_in, 16 * (t + 1))
                    pool.sem_inc(part_free, 1)
                    for f in range(lo, hi):
                        gather(f, part)

        @block.scalar
        def _(act):
            act.sem_inc(hidden_ready, 2)
            act.sem_inc(kept, 2 * CHUNKS)

            def relu(s, j):
                act.wait_ge(scored, s + 1)
                for w in range(WAVES):
                    pair = (WAVES * j + w) % 2
                    act.wait_ge(raw_ready, WAVES * (s + 2) + w + 1)
                    act.activation(
                        hidden[j][:, 2 * BLOCK_COLS * w:2 * BLOCK_COLS * (w + 1)
                                       ].rearrange("p (c n) -> p c n", c=2),
                        raw[:, 2 * pair:2 * pair + 2, 0:BLOCK_COLS], ACT.Relu, bias=attn_bias[:, 0:1]
                    ).then_inc(hidden_ready, 1)

            def exp(t):
                positive(act, folded_ready, t)
                act.wait_ge(max_ready, t + 1)
                act.activation(skew_write[:, 1:SHIFTS + 1, :].rearrange("p (h s) i -> p h s i", h=2),
                               scores[:, :, 0:HALF].rearrange("p h (s i) -> p h s i", i=F), ACT.Exp,
                               bias=neg_max[:, 0:1], accum_out=row_sum[:, 0:1]).then_inc(exp_ready, 1)

            def chunk_of_xt(parity, c):
                return xt[:, parity].rearrange("p (q c r) f -> p c q r f", q=Q, r=R)[:, bass.ds(c, 1)].rearrange(
                    "p one q r f -> p (one q) r f")

            def keep_turned(v, parity, c, again):
                if again:
                    act.wait_ge(mix_taken, v - 2 * CHUNKS + 2)
                act.wait_ge(turned, 2 * v + 1)
                at = chunk_of_xt(parity, c)
                fields = turn_bank[:].rearrange("p (q r f) -> p q r f", q=Q, f=FM)
                act.activation(at[:, :, :, F:FX], fields[:, :, :, 0:SHIFTS], ACT.Copy)
                act.activation(at[:, :, :, 0:FM], fields, ACT.Copy).then_inc(kept, 1)

            def keep_last(v, parity, c):
                act.wait_ge(turned, 2 * v + 2)
                act.activation(chunk_of_xt(parity, c)[:, :, :, FM],
                               turn_bank[:, 0:Q * R].rearrange("p (q r) -> p q r", q=Q), ACT.Copy
                               ).then_inc(kept, 1)

            def two_chunks(t, parity, c, half, mixes, turns, softmax=False):
                for k in range(2):
                    n = CHUNKS * t + c + k
                    to = (n + TURN_AHEAD, (parity, 1 - parity)[half], c + k + (TURN_AHEAD, TURN_AHEAD - CHUNKS)[half])
                    for j in range(R):
                        relu(R * n + j, j)
                        if turns and j == 1:
                            keep_turned(*to, again=mixes)
                        if softmax and k == 0 and j == 2:
                            exp(t - 1)
                        if turns and j == 3:
                            keep_last(*to)

            def tile(t, parity, mixes=(True, True), turns=(True, True)):
                two_chunks(t, parity, 0, 0, mixes[0], turns[0], softmax=type(t) is not int or t > 0)
                two_chunks(t, parity, 2, 0, mixes[0], turns[0])
                with act.Fori(TURN_AHEAD, CHUNKS - 1, 2) as c:
                    two_chunks(t, parity, c, 1, mixes[1], turns[1])

            act.wait_ge(weights_in, 16 * WEIGHTS)
            act.activation(row_sum[:], attn_bias[:], ACT.Exp)
            for g, (part, lo, hi) in enumerate(FIELD_GROUPS):
                act.wait_ge(fields_turned, g + 1)
                fields = raw[:, g % 4, 0:TILE * (hi - lo)].rearrange("p (f b) -> p f b", b=TILE)
                again = max(min(hi, SHIFTS) - lo, 0)
                if again:
                    act.activation(xt[:, 0].rearrange("p b f -> p f b")[:, F + lo:F + lo + again],
                                   fields[:, 0:again], ACT.Copy)
                act.activation(xt[:, 0].rearrange("p b f -> p f b")[:, lo:hi], fields, ACT.Copy
                               ).then_inc(fields_kept, 1)
            act.wait_ge(start_kept, START)
            act.wait_ge(skewed_zeroed, 1)
            all_tiles(act, tile)
            exp(TILES - 1)

            for n, (layer, blk, c) in enumerate(TOWER):
                bank = raw[:, n % 4, :]
                if layer == 1:
                    act.wait_ge(l1_summed, L1 * blk + c + 1)
                    act.activation(h1[:, c, :], h1[:, c, :], ACT.Relu).then_inc(tower_taken, 1)
                elif layer == 2:
                    act.wait_ge(tower_ready, n + 1)
                    act.activation(h2[:, c, :], bank, ACT.Relu, bias=b2_sb[:, c:c + 1]).then_inc(tower_taken, 1)
                else:
                    act.wait_ge(tower_ready, n + 1)
                    act.activation(y_row[0:1, blk * BLOCK:(blk + 1) * BLOCK], bank[0:1], ACT.Copy
                                   ).then_inc(tower_taken, 1)

        @block.vector
        def _(dve):
            dve.sem_inc(mix_taken, 1)
            dve.sem_inc(ao_ready, 2)
            dve.memset(onehot[:], 0.0).then_inc(onehot_made, 1)
            dve.memset(zeros[:], 0.0).then_inc(onehot_made, 1)
            dve.wait_ge(onehot_made, 1)
            dve.memset(onehot[:, QCOLS:QCOLS + 1], 1.0).then_inc(onehot_made, 1)
            for n in range(START):
                dve.wait_ge(start_turned, n + 1)
                dst = attn_wt[:] if n == 0 else gt[:, (n - 1) * TILE:n * TILE]
                dve.tensor_copy(dst, (mix_bank, turn_bank)[n % 2][:, 0:TILE]).then_inc(start_kept, 1)
            dve.wait_ge(weights_in, 16 * WEIGHTS)
            dve.tensor_tensor(w1_gnn[:], w1_sb[:, 0, :], w1_sb[:, 2, :], ALU.add).then_inc(w1_added, 1)
            dve.wait_ge(onehot_made, 3)
            for n in range(BLOCKS * L1):
                dve.wait_ge(l1_product, n + 1)
                dve.tensor_scalar(l1_made[:, n * BLOCK:(n + 1) * BLOCK], (mix_bank, turn_bank)[n % 2][:, 0:BLOCK],
                                  b1_sb[:, n % L1:n % L1 + 1], None, ALU.add).then_inc(l1_kept, 1)
            dve.wait_ge(start_kept, START)
            dve.wait_ge(fields_kept, len(FIELD_GROUPS))

            def multiply(s, m, tile_parity, parity):
                dve.wait_ge(raw_ready, WAVES * (s + 1))
                row = xt[:, tile_parity, bass.ds(m, 1), 0:F]
                at, step_q = row.offset, QCOLS * FX
                left = bass.AP(row.tensor, at, [row.ap[0], [step_q, Q], [0, SHIFTS], [1, F]])
                right = bass.AP(row.tensor, at + 1, [row.ap[0], [step_q, Q], [1, SHIFTS], [1, F]])
                dve.tensor_tensor(products[parity][:].rearrange("p (q s i) -> p q s i", q=Q, i=F),
                                  left, right, ALU.mult).then_inc(products_ready, 1)

            def place_g(s, t, m, j):
                dve.wait_ge(scored, s + 1)
                g4 = gt[:, bass.ds(t * TILE + m, 1)]
                g4 = bass.AP(g4.tensor, g4.offset, [g4.ap[0], [QCOLS, Q], [0, QCOLS]])
                hot = onehot[:, bass.ds(QCOLS - m, QCOLS)]
                hot = bass.AP(hot.tensor, hot.offset, [hot.ap[0], [0, Q], [1, QCOLS]])
                dve.tensor_tensor(g_col[j][:], g4, hot, ALU.mult).then_inc(g_ready, 1)

            def find_max(t):
                dve.wait_ge(scored, R + STEPS * (t + 1))
                positive(dve, exp_ready, t)
                dve.tensor_reduce(row_max[:], scores[:, :, 0:HALF], AX.XY, ALU.max).then_inc(max_found, 1)
                dve.wait_ge(max_found, t + 1)
                dve.tensor_scalar(neg_max[:], row_max[:], -1.0, None, ALU.mult).then_inc(max_ready, 1)

            def fold(t):
                dve.wait_ge(exp_ready, t + 1)
                dve.reciprocal(inv_sum[:], row_sum[:]).then_inc(fold_step, 1)
                dve.wait_ge(fold_step, 3 * t + 1)
                dve.tensor_scalar(inv_sum100[:], inv_sum[:], 100.0, None, ALU.mult).then_inc(fold_step, 1)
                positive(dve, w_stored, 16 * t)
                dve.wait_ge(fold_step, 3 * t + 2)
                dve.tensor_scalar(folded[:], skew_read[:, 0:FM, 1:F], inv_sum100[:, 0:1], None, ALU.mult
                                  ).then_inc(fold_step, 1)
                dve.wait_ge(fold_step, 3 * t + 3)
                wrapped = skew_read[:, F - SHIFTS:F, F:FX].rearrange("p k i -> p i k")
                dve.scalar_tensor_tensor(out=folded[:, 0:SHIFTS, FM - SHIFTS:FM], in0=wrapped,
                                         scalar=inv_sum100[:, 0:1], in1=folded[:, 0:SHIFTS, FM - SHIFTS:FM],
                                         op0=ALU.mult, op1=ALU.add).then_inc(folded_ready, 1)

            def finish_mix(u, t, parity, c, k, bank=mix_bank):
                dve.wait_ge(mix_ready, u + 3)
                dve.wait_ge(ao_ready, u + 1)
                right = xt[:, parity].rearrange("p (q c r) f -> p c q r f", q=Q, r=R)[:, bass.ds(c, 1)].rearrange(
                    "p one q r f -> p (one q) r f")[:, :, :, 1:F]
                dve.tensor_tensor(mixed[k][:], bank[:].rearrange("p (q r f) -> p q r f", q=Q, f=FM),
                                  right, ALU.mult).then_inc(mix_taken, 1)
                dve.wait_ge(mix_taken, u + 2)
                out = ao[:, bass.ds(t * TILE + R * c, 1)]
                out = bass.AP(out.tensor, out.offset, [out.ap[0], [QCOLS, Q], [1, R]])
                dve.tensor_reduce(out, mixed[k][:], AX.X, ALU.add).then_inc(ao_ready, 1)

            def two_chunks(t, parity, c, half, mixes, softmax=False):
                for k in range(2):
                    n = CHUNKS * t + c + k
                    dve.wait_ge(kept, 2 * (n + 1))
                    for j in range(R):
                        m = R * (c + k) + j
                        multiply(STEPS * t + m, m, parity, j % 2)
                        place_g(STEPS * t + m, t, m, j)
                        if softmax and k == 0 and j == 3:
                            find_max(t - 1)
                        if mixes and j == 1:
                            finish_mix(n - MIX_BEHIND, t - 2 + half, (parity, 1 - parity)[half],
                                       c + k + (TURN_AHEAD, -TURN_AHEAD)[half], k)

            def tile(t, parity, mixes=(True, True), turns=(True, True)):
                later = type(t) is not int or t > 0
                two_chunks(t, parity, 0, 0, mixes[0], softmax=later)
                if later:
                    fold(t - 1)
                two_chunks(t, parity, 2, 0, mixes[0])
                with dve.Fori(TURN_AHEAD, CHUNKS - 1, 2) as c:
                    two_chunks(t, parity, c, 1, mixes[1])

            all_tiles(dve, tile)
            find_max(TILES - 1)
            for n, (layer, blk, c) in enumerate(TOWER):
                if layer == 1:
                    if c == 0:
                        dve.wait_ge(l1_loaded[blk], 16)
                    dve.wait_ge(tower_ready, n + 1)
                    dve.tensor_tensor(h1[:, c, :], raw[:, n % 4, :], l1_gnn[blk][:, BLOCK * c:BLOCK * (c + 1)],
                                      ALU.add).then_inc(l1_summed, 1)
                if n == L1 - 1:
                    fold(TILES - 1)
                for u in late_mixes(n):
                    finish_mix(u, u // CHUNKS, u // CHUNKS % 2, u % CHUNKS, u % 2, (turn_bank, mix_bank)[u % 2])

        @block.tensor
        def _(pe):
            pe.sem_inc(raw_ready, 2 * WAVES)
            pe.sem_inc(mix_ready, 2)
            pe.sem_inc(scored, R)
            pe.sem_inc(turned, 2 * CHUNKS)

            def turn(v, pairs, k):
                pe.wait_ge(turn_loaded[k], 32 * (pairs + 1))
                pe.wait_ge(kept, 2 * v)
                for q in range(Q):
                    last = pe.transpose(turn_bank[:, P * q:P * (q + 1)], x_turn[k][:, q, :], ident[:])
                last.then_inc(turned, 1)

            def turn_last(v, k):
                pe.wait_ge(kept, 2 * v + 1)
                pe.sem_inc(last_turns, 1)
                pe.transpose(turn_bank[:, 0:Q * R], x_turn_last[k][:], ident[0:Q * R, 0:Q * R]
                             ).then_inc(turned, 1)

            def mix(u, pairs, t, parity, c, k, bank=mix_bank, taken=1):
                pe.wait_ge(w_loaded, 16 * R * (t + 1))
                pe.wait_ge(mix_loaded[k], 16 * (pairs + 1))
                pe.wait_ge(mix_taken, u + taken)
                for q in range(Q):
                    last = pe.matmul(bank[:, P * q:P * (q + 1)], x_mix[k][:, q, :],
                                     w_rows[:, parity, bass.ds(CHUNKS * q + c, 1), :].rearrange(
                                         "p one n -> p (one n)"), start=True, stop=True)
                last.then_inc(mix_ready, 1)

            def hide(s, parity):
                pe.wait_ge(products_ready, s + 1)
                for w in range(WAVES):
                    pair = (WAVES * parity + w) % 2
                    pe.wait_ge(hidden_ready, WAVES * s + w + 1)
                    for c in range(2):
                        at = (2 * w + c) * BLOCK_COLS
                        last = pe.matmul(raw[:, 2 * pair + c, 0:BLOCK_COLS], attn_wt[:],
                                         products[parity][:, at:at + BLOCK_COLS], start=True, stop=True)
                    last.then_inc(raw_ready, 1)

            def score(s, j):
                pe.wait_ge(g_ready, s + 1)
                pe.wait_ge(hidden_ready, 2 + WAVES * (s + 1))
                for h in range(2):
                    for q in range(Q):
                        at = q * PAIRS + h * HALF
                        last = pe.matmul(scores[QCOLS * q:QCOLS * (q + 1), h, 0:HALF], g_col[j][:, q, :],
                                         hidden[j][:, at:at + HALF], start=False, stop=False,
                                         skip_group_check=True)
                last.then_inc(scored, 1)

            def clear_scores(t):
                positive(pe, exp_ready, t)
                for h in range(2):
                    pe.matmul(scores[:, h, 0:HALF], zeros[:, 0:P], zeros[:], start=True, stop=False,
                              skip_group_check=True)

            def two_chunks(t, parity, c, pairs, half, mixes, turns, head=False):
                for k in range(2):
                    n = CHUNKS * t + c + k
                    for j in range(R):
                        hide(R * n + j, j % 2)
                        if turns and j == 2:
                            turn_last(n + TURN_AHEAD, k)
                        if j == 1 and not (head and k == 0 and type(t) is int and t == 0):
                            score(R * n - 2, 2)
                            score(R * n - 1, 3)
                        if j == 3:
                            if head and k == 0:
                                clear_scores(t)
                            score(R * n, 0)
                            score(R * n + 1, 1)
                        if mixes and j == 0:
                            mix(n - MIX_BEHIND, pairs - MIX_BEHIND // 2, t - 2 + half, (parity, 1 - parity)[half],
                                c + k + (TURN_AHEAD, -TURN_AHEAD)[half], k)
                        if turns and j == 1:
                            turn(n + TURN_AHEAD, pairs + (TURN_AHEAD - CHUNKS) // 2, k)

            def tile(t, parity, mixes=(True, True), turns=(True, True)):
                pairs = CHUNKS // 2 * t
                two_chunks(t, parity, 0, pairs, 0, mixes[0], turns[0], head=True)
                two_chunks(t, parity, 2, pairs + 1, 0, mixes[0], turns[0])
                with pe.Fori(TURN_AHEAD // 2, CHUNKS // 2) as pair:
                    two_chunks(t, parity, 2 * pair, pairs + pair, 1, mixes[1], turns[1])

            pe.wait_ge(constants, 2)
            pe.wait_ge(start_in, 2 * 16)
            for n in range(START):
                if n >= 2:
                    pe.wait_ge(start_kept, n - 1)
                pe.transpose((mix_bank, turn_bank)[n % 2][:, 0:TILE],
                             attn_w_rows if n == 0 else g_rows[:, n - 1, :], ident[:]).then_inc(start_turned, 1)
            pe.wait_ge(start_kept, START)
            pe.wait_ge(w1_added, 1)

            def share_of_g(n):
                blk, c = n // L1, n % L1
                positive(pe, l1_kept, n - 1)
                pe.matmul((mix_bank, turn_bank)[n % 2][:, 0:BLOCK], w1_gnn[:, c * P:(c + 1) * P],
                          gt[:, blk * BLOCK:(blk + 1) * BLOCK], start=True, stop=True).then_inc(l1_product, 1)

            def turn_fields(these):
                pe.wait_ge(gathered[these], 16 * (PARTS[these][1] - PARTS[these][0]))
                for g, (part, lo, hi) in enumerate(FIELD_GROUPS):
                    if part == these:
                        positive(pe, fields_kept, g - 3)
                        for f in range(lo, hi):
                            last = pe.transpose(raw[:, g % 4, TILE * (f - lo):TILE * (f - lo + 1)], x_b[:, f, :],
                                                ident[:])
                        last.then_inc(fields_turned, 1)

            for n in range(BLOCKS * L1):
                if n == BLOCKS * L1 // 2:
                    turn_fields(0)
                share_of_g(n)
            for part in range(1, len(PARTS)):
                turn_fields(part)
            pe.wait_ge(onehot_made, 3)
            all_tiles(pe, tile)
            score(STEPS * TILES - 2, 2)
            score(STEPS * TILES - 1, 3)
            for n, (layer, blk, c) in enumerate(TOWER):
                cols = slice(blk * BLOCK, (blk + 1) * BLOCK)
                bank = raw[:, n % 4, :]
                positive(pe, tower_taken, n - 3)
                if layer == 1:
                    if c == 0:
                        pe.wait_ge(ao_ready, 2 + (blk + 1) * ALL_CHUNKS // BLOCKS)
                    last = pe.matmul(bank, w1_sb[:, 1, c * P:(c + 1) * P], ao[:, cols], start=True, stop=True)
                elif layer == 2:
                    pe.wait_ge(tower_taken, TOWER.index((1, blk, L1 - 1)) + 1)
                    for j in range(L1):
                        last = pe.matmul(bank, w2_sb[:, j, c * P:(c + 1) * P], h1[:, j, :],
                                         start=(j == 0), stop=(j == L1 - 1))
                else:
                    pe.wait_ge(tower_taken, TOWER.index((2, blk, L2 - 1)) + 1)
                    for j in range(L2):
                        last = pe.matmul(bank[0:1], w3_sb[:, j:j + 1], h2[:, j, :],
                                         start=(j == 0), stop=(j == L2 - 1))
                last.then_inc(tower_ready, 1)
                for u in late_mixes(n):
                    mix(u, u // 2, u // CHUNKS, u // CHUNKS % 2, u % CHUNKS, u % 2,
                        bank=(turn_bank, mix_bank)[u % 2], taken=0)


def kernel(**inputs):
    import numpy as np
    import concourse.bacc as bacc
    from concourse.bass_utils import run_bass_kernel_spmd

    nc = bacc.Bacc("TRN2", target_bir_lowering=False, num_devices=1)
    arrays = {}

    def given(name):
        a = np.ascontiguousarray(inputs[name])
        arrays[f"in_{name}"] = a
        return nc.dram_tensor(f"in_{name}", a.shape, mybir.dt.from_np(a.dtype), kind="ExternalInput").ap()

    gnn, ids = given("r_gnn_feature"), given("ids")
    tables = [given(f"tbl_{f}") for f in range(F)]
    rest = [given(n) for n in ("W_top1", "b_top1", "W_top2", "b_top2", "W_top3", "L0_rec_attn_W", "L0_rec_attn_b")]
    y = nc.dram_tensor("out_y", (B, 1), F32, kind="ExternalOutput").ap()
    build(nc, gnn, ids, tables, *rest, y)
    result = run_bass_kernel_spmd(nc, [arrays], core_ids=[0])
    return result.results[0]["out_y"]
```
